# Optimizing a Trainium2 kernel written in Bass

```python
import numpy as np
import jax
import jax.numpy as jnp

def _softmax(x, axis=-1):
    return jax.nn.softmax(x, axis=axis)

def _gelu(x):
    return jax.nn.gelu(x, approximate=True)

def _silu(x):
    return jax.nn.silu(x)

def _sigmoid(x):
    return jax.nn.sigmoid(x)

def _layernorm(x, axis=-1, eps=1e-05):
    m = jnp.mean(x, axis=axis, keepdims=True)
    v = jnp.var(x, axis=axis, keepdims=True)
    return (x - m) / jnp.sqrt(v + eps)

def _scatter_add(tgt, idx, src, axis=0):
    return tgt.at[idx].add(src)

def _segment_sum(src, seg, n):
    return jax.ops.segment_sum(src, seg, n)
kernel_name = 'mk_rec_standalone_d1_rec_r8_160355'

def setup_inputs(seed: int=0):
    np.random.seed(seed)
    _w = jnp.asarray

    def _rec_inputs():
        import jax
        import jax.numpy as jnp
        _rk = jax.random.key(seed)
        r_x = jax.random.bernoulli(jax.random.fold_in(_rk, 1), 0.0009984, (512, 10202)).astype(jnp.float32)
        return r_x
    r_x = _rec_inputs()

    def _L0_rec_setup():
        import jax, jax.numpy as jnp
        import numpy as np
        VOCAB = 10202
        DIM = 32
        BATCH = 512
        key = jax.random.key(seed)
        k1, k2 = jax.random.split(key)
        x = (jax.random.uniform(k1, (BATCH, VOCAB), dtype=jnp.float32) < 0.001).astype(jnp.float32)
        w = jax.random.normal(k2, (VOCAB, DIM), dtype=jnp.float32) * 0.05
        b = jnp.zeros((DIM,), dtype=jnp.float32)
        return {'x': x, 'w': w, 'b': b}
    _L0_rec_all = _L0_rec_setup()
    _L0_rec_in = {k: v for k, v in _L0_rec_all.items() if k in ('w', 'b')}
    del _L0_rec_all
    return {'r_x': r_x, 'L0_rec_w': _L0_rec_in['w'], 'L0_rec_b': _L0_rec_in['b']}

def reference(r_x, L0_rec_w, L0_rec_b):
    import jax
    import jax.numpy as jnp

    def _L0_rec_ref(x, w, b):
        import jax, jax.numpy as jnp
        import numpy as np
        VOCAB = 10202
        DIM = 32
        BATCH = 512
        h = jax.nn.sigmoid(x @ w + b)
        y_pred = jax.nn.sigmoid(h @ w.T)
        return y_pred
    y = _L0_rec_ref(r_x, L0_rec_w, L0_rec_b)
    return y

_drawn_inputs = setup_inputs


def setup_inputs(seed=0):
    import zlib

    import numpy as np

    out = dict(_drawn_inputs(seed))
    spreads = {'L0_rec_b': (0.0, 2.0)}
    factors = {'r_x': 8.0}
    for name, (base, spread) in spreads.items():
        noise = np.random.default_rng([zlib.crc32(name.encode()), seed]).standard_normal(out[name].shape)
        drawn = base * np.exp(spread * noise) if base else spread * noise
        out[name] = jnp.asarray(drawn.astype(out[name].dtype))
    for name, factor in factors.items():
        out[name] = (out[name] * factor).astype(out[name].dtype)
    return out
```

```python
from contextlib import ExitStack

import concourse.bass as bass
from concourse import mybir

P = 128
GROUPS = 4
D = 32
BATCH, VOCAB = 512, 10202
HALVES = 2
HB = BATCH // HALVES
TILES = -(-VOCAB // P)
FULL = TILES - 1
TAIL = VOCAB - FULL * P
CHUNK = 8
CHUNKS = TILES // CHUNK
BANK = 512
ROUND = GROUPS * BANK
ROUNDS = -(-VOCAB // ROUND)
BTILES = HB // P
SLOTS = BTILES * ROUNDS
PAIR = 2
PAIRS = SLOTS * GROUPS // PAIR
PAIR_BUFFERS = 3
assert CHUNKS * CHUNK == TILES and TILES * P == ROUNDS * ROUND

F32 = mybir.dt.float32
ALU = mybir.AluOpType
ACT = mybir.ActivationFunctionType


def tile_order():
    per_bank = BANK // P
    return [ROUND // P * q + per_bank * r + j
            for q in range(ROUNDS) for j in range(per_bank) for r in range(GROUPS)]


def autoencoder(nc, x_main, x_tail, w_main, w_tail, bias, y):
    place = {tile: n for n, tile in enumerate(tile_order())}

    with ExitStack() as ctx:
        def sb(name, shape):
            return ctx.enter_context(nc.sbuf_tensor(name, shape, F32))

        def psum(name, shape):
            return ctx.enter_context(nc.psum_tensor(name, shape, F32))

        def sem(name):
            return ctx.enter_context(nc.semaphore(name))

        x_sb = sb("x_sb", [P, CHUNKS, CHUNK * HB])
        y_sb = sb("y_sb", [P, SLOTS, ROUND])
        w_sb = sb("w_sb", [P, TILES * D])
        wT_sb = sb("wT_sb", [P, ROUNDS * BANK])
        partial_sb = sb("partial_sb", [P, HB])
        hT_sb = sb("hT_sb", [P, HB])
        bias_sb = sb("bias_sb", [P, 1])
        ident = sb("ident", [P, P])
        join = sb("join", [P, P])

        logits_ps = psum("logits_ps", [P, PAIR_BUFFERS, PAIR, BANK])
        partial_ps = psum("partial_ps", [P, BANK])
        total_ps = psum("total_ps", [P, BANK])

        w_loaded = sem("w_loaded")
        w_tail_cleared = sem("w_tail_cleared")
        bias_loaded = sem("bias_loaded")
        x_loaded = [sem(f"x_loaded{c}") for c in range(CHUNKS)]
        masks_cleared = sem("masks_cleared")
        masks_step = sem("masks_step")
        transposed = sem("transposed")
        wT_copied = sem("wT_copied")
        x_used = sem("x_used")
        partial_copied = sem("partial_copied")
        total_ready = sem("total_ready")
        hT_ready = sem("hT_ready")
        logits_ready = sem("logits_ready")
        y_ready = sem("y_ready")
        y_stored = [sem(f"y_stored{k}") for k in range(SLOTS)]

        MASK_STEPS = 1 + GROUPS
        X_DMAS = [1] * (CHUNKS - 1) + [2]

        block = ctx.enter_context(nc.Block())

        @block.sync
        def _(sp):
            sp.dma_start(w_sb[:, 0:FULL * D], w_main[:, :]).then_inc(w_loaded, 16)
            with sp.Fori(0, HALVES) as half:
                for c in range(CHUNKS):
                    sp.wait_ge(x_used, half * (c + 1))
                    first, last = c * CHUNK, min((c + 1) * CHUNK, FULL)
                    sp.dma_start(x_sb[:, c, 0:(last - first) * HB],
                                 x_main[half, :, first * HB:last * HB]).then_inc(x_loaded[c], 16)
                sp.dma_start(x_sb[0:TAIL, CHUNKS - 1, (CHUNK - 1) * HB:CHUNK * HB],
                             x_tail[half, :, :]).then_inc(x_loaded[CHUNKS - 1], 16)
            with sp.Fori(0, HALVES) as half:
                for k in range(SLOTS):
                    btile, q = divmod(k, ROUNDS)
                    width = min(ROUND, VOCAB - q * ROUND)
                    sp.wait_ge(y_ready, half * PAIRS + (k + 1) * (PAIRS // SLOTS))
                    sp.dma_start(y[half, btile, :, q * ROUND:q * ROUND + width],
                                 y_sb[:, k, 0:width]).then_inc(y_stored[k], 16)
            for k in range(SLOTS):
                sp.wait_ge(y_stored[k], 16 * HALVES)

        @block.gpsimd
        def _(pool):
            pool.memset(w_sb[:, FULL * D:TILES * D], 0.0).then_inc(w_tail_cleared, 1)
            pool.memset(ident[:, :], 0.0).then_inc(masks_cleared, 1)
            pool.memset(join[:, :], 0.0).then_inc(masks_cleared, 1)
            pool.wait_ge(masks_cleared, 2)
            pool.affine_select(out=ident[:, :], in_=ident[:, :], compare_op=ALU.not_equal, fill=1.0,
                               base=0, pattern=[[-1, P]], channel_multiplier=1).then_inc(masks_step, 1)
            join_v = join[:, :].rearrange("p (g d) -> p g d", g=GROUPS)
            for g in range(GROUPS):
                pool.wait_ge(masks_step, g + 1)
                pool.affine_select(out=join_v, in_=join_v, compare_op=ALU.not_equal, fill=1.0,
                                   base=-g * D, pattern=[[0, GROUPS], [-1, D]],
                                   channel_multiplier=1).then_inc(masks_step, 1)

        @block.tensor
        def _(pe):
            pe.wait_ge(masks_step, MASK_STEPS)
            pe.wait_ge(w_loaded, 32)
            for q in range(ROUNDS):
                for j in range(BANK // P):
                    n = q * (BANK // P) + j
                    last = nc.tensor.transpose(logits_ps[:, q // PAIR, q % PAIR, j * P:(j + 1) * P],
                                               w_sb[:, n * P:(n + 1) * P], ident[:, :])
                last.then_inc(transposed, 1)

            with pe.Fori(0, HALVES) as half:
                for c in range(CHUNKS):
                    pe.wait_ge(x_loaded[c], (half + 1) * (16 * X_DMAS[c]))
                    for i in range(CHUNK):
                        t = c * CHUNK + i
                        g, rows = t % GROUPS, P if t < FULL else TAIL
                        last = nc.tensor.matmul(partial_ps[g * D:(g + 1) * D, 0:HB],
                                                w_sb[0:rows, place[t] * D:(place[t] + 1) * D],
                                                x_sb[0:rows, c, i * HB:(i + 1) * HB],
                                                start=t < GROUPS, stop=t >= TILES - GROUPS)
                    last.then_inc(x_used, 1)
                pe.wait_ge(partial_copied, half + 1)
                nc.tensor.matmul(total_ps[:, 0:HB], join[:, :], partial_sb[:, :],
                                 start=True, stop=True).then_inc(total_ready, 1)
                pe.wait_ge(wT_copied, ROUNDS)
                pe.wait_ge(hT_ready, half + 1)
                for pair in range(PAIRS):
                    k, r0 = divmod(pair * PAIR, GROUPS)
                    btile, q = divmod(k, ROUNDS)
                    pe.wait_ge(y_ready, half * PAIRS + max(pair - PAIR_BUFFERS + 1, 0))
                    for i in range(PAIR):
                        rows = slice((r0 + i) * D, (r0 + i + 1) * D)
                        last = nc.tensor.matmul(logits_ps[:, pair % PAIR_BUFFERS, i, :],
                                                hT_sb[rows, btile * P:(btile + 1) * P],
                                                wT_sb[rows, q * BANK:(q + 1) * BANK],
                                                start=True, stop=True)
                    last.then_inc(logits_ready, 1)

        @block.vector
        def _(dve):
            for q in range(ROUNDS):
                dve.wait_ge(transposed, q + 1)
                nc.vector.tensor_copy(wT_sb[:, q * BANK:(q + 1) * BANK],
                                      logits_ps[:, q // PAIR, q % PAIR, :]).then_inc(wT_copied, 1)
            with dve.Fori(0, HALVES) as half:
                dve.wait_ge(x_used, (half + 1) * CHUNKS)
                nc.vector.tensor_copy(partial_sb[:, :], partial_ps[:, 0:HB]).then_inc(partial_copied, 1)

        @block.scalar
        def _(act):
            act.wait_ge(w_tail_cleared, 1)
            act.dma_start(w_sb[0:TAIL, FULL * D:TILES * D], w_tail[:, :]).then_inc(w_loaded, 16)
            for g in range(GROUPS):
                act.dma_start(bias_sb[g * D:(g + 1) * D, :], bias[:, :]).then_inc(bias_loaded, 16)
            act.wait_ge(bias_loaded, 16 * GROUPS)
            with act.Fori(0, HALVES) as half:
                act.wait_ge(total_ready, half + 1)
                nc.scalar.activation(hT_sb[:, :], total_ps[:, 0:HB], ACT.Sigmoid,
                                     bias=bias_sb[:, 0:1]).then_inc(hT_ready, 1)
                for pair in range(PAIRS):
                    k, r0 = divmod(pair * PAIR, GROUPS)
                    if r0 == 0:
                        act.wait_ge(y_stored[k], half * 16)
                    act.wait_ge(logits_ready, half * PAIRS + (pair + 1))
                    nc.scalar.activation(y_sb[:, k, r0 * BANK:(r0 + PAIR) * BANK],
                                         logits_ps[:, pair % PAIR_BUFFERS, :, :],
                                         ACT.Sigmoid).then_inc(y_ready, 1)


def kernel(r_x, L0_rec_w, L0_rec_b):
    import numpy as np
    import concourse.bacc as bacc
    from concourse.bass_utils import run_bass_kernel_spmd

    x, w, b = (np.asarray(a) for a in (r_x, L0_rec_w, L0_rec_b))
    x_main = x[:, :FULL * P].reshape(HALVES, HB, FULL, P).transpose(0, 3, 2, 1)
    x_tail = x[:, FULL * P:].reshape(HALVES, HB, TAIL).transpose(0, 2, 1)
    w_main = w[:FULL * P].reshape(FULL, P, D)[tile_order()[:FULL]].transpose(1, 0, 2)
    arrays = {
        "x_main": np.ascontiguousarray(x_main).reshape(HALVES, P, FULL * HB),
        "x_tail": np.ascontiguousarray(x_tail),
        "w_main": np.ascontiguousarray(w_main).reshape(P, FULL * D),
        "w_tail": np.ascontiguousarray(w[FULL * P:]),
        "bias": b.reshape(D, 1),
    }
    nc = bacc.Bacc("TRN2", target_bir_lowering=False, num_devices=1)
    ins = [nc.dram_tensor(name, a.shape, F32, kind="ExternalInput").ap() for name, a in arrays.items()]
    y = nc.dram_tensor("y", (HALVES, BTILES, P, VOCAB), F32, kind="ExternalOutput").ap()
    autoencoder(nc, *ins, y)
    r = run_bass_kernel_spmd(nc, [arrays], core_ids=[0])
    return r.results[0]["y"].reshape(BATCH, VOCAB)
```

```python
from contextlib import ExitStack

import concourse.bass as bass
from concourse import mybir

P = 128
GROUPS = 4
D = 32
PARTS = 3
BATCH, VOCAB = 512, 10202
HALVES = 2
HB = BATCH // HALVES
TILES = -(-VOCAB // P)
FULL = TILES - 1
TAIL = VOCAB - FULL * P
CHUNK = 8
CHUNKS = TILES // CHUNK
BANK = 512
PAIR = 2
PAIR_BUFFERS = 2
ROUND = 2 * PAIR * BANK
ROUNDS = -(-VOCAB // ROUND)
PAIRS = ROUND // (PAIR * BANK)
TURN = ROUND // P
BTILES = HB // P
SLOTS = BTILES * ROUNDS
SPLIT_STEPS = 4
assert CHUNKS * CHUNK == TILES == ROUNDS * TURN

F32 = mybir.dt.float32
BF16 = mybir.dt.bfloat16
ALU = mybir.AluOpType
ACT = mybir.ActivationFunctionType


def autoencoder(nc, x_main, x_tail, w_main, w_tail, bias, y):
    with ExitStack() as ctx:
        def sb(name, shape, dt=F32):
            return ctx.enter_context(nc.sbuf_tensor(name, shape, dt))

        def psum(name, shape):
            return ctx.enter_context(nc.psum_tensor(name, shape, F32))

        def sem(name):
            return ctx.enter_context(nc.semaphore(name))

        x_sb = sb("x_sb", [P, CHUNKS, CHUNK * HB])
        y_sb = sb("y_sb", [P, SLOTS, ROUND])
        w_sb = sb("w_sb", [P, TILES * D])
        w_rest = sb("w_rest", [P, TURN, D])
        w_parts = sb("w_parts", [P, TURN, PARTS * D], BF16)
        wT_parts = sb("wT_parts", [PARTS * D, TILES * P], BF16)
        partial_sb = sb("partial_sb", [P, HB])
        h_sb = sb("h_sb", [PARTS * D, HB])
        h_rest = sb("h_rest", [PARTS * D, HB])
        h_parts = sb("h_parts", [PARTS * D, PARTS, HB], BF16)
        bias_sb = sb("bias_sb", [PARTS * D, 1])
        ident = sb("ident", [P, P], BF16)
        join = sb("join", [P, PARTS * D])

        logits_ps = psum("logits_ps", [P, PAIR_BUFFERS, PAIR, BANK])
        turned_ps = psum("turned_ps", [P, PAIR * BANK])
        partial_ps = psum("partial_ps", [P, BANK])
        total_ps = psum("total_ps", [P, BANK])

        w_loaded = sem("w_loaded")
        w_tail_loaded = sem("w_tail_loaded")
        w_tail_cleared = sem("w_tail_cleared")
        bias_loaded = sem("bias_loaded")
        x_loaded = [sem(f"x_loaded{c}") for c in range(CHUNKS)]
        masks_cleared = sem("masks_cleared")
        masks_step = sem("masks_step")
        w_split = sem("w_split")
        w_parts_free = sem("w_parts_free")
        turned_free = sem("turned_free")
        x_free = sem("x_free")
        partial_copied = sem("partial_copied")
        total_ready = sem("total_ready")
        h_ready = sem("h_ready")
        h_split = sem("h_split")
        logits_ready = sem("logits_ready")
        logits_free = sem("logits_free")
        y_stored = [sem(f"y_stored{q}") for q in range(ROUNDS)]

        MASK_STEPS = 1 + GROUPS
        X_DMAS = [1] * (CHUNKS - 1) + [2]

        block = ctx.enter_context(nc.Block())

        @block.sync
        def _(sp):
            sp.dma_start(w_sb[:, 0:FULL * D], w_main[:, :]).then_inc(w_loaded, 16)
            sp.sem_inc(x_free, CHUNKS)
            with sp.Fori(0, HALVES) as half:
                for c in range(CHUNKS):
                    sp.wait_ge(x_free, half * CHUNKS + (c + 1))
                    first, last = c * CHUNK, min((c + 1) * CHUNK, FULL)
                    sp.dma_start(x_sb[:, c, 0:(last - first) * HB],
                                 x_main[half, :, first * HB:last * HB]).then_inc(x_loaded[c], 16)
                sp.dma_start(x_sb[0:TAIL, CHUNKS - 1, (CHUNK - 1) * HB:CHUNK * HB],
                             x_tail[half, :, :]).then_inc(x_loaded[CHUNKS - 1], 16)
            for half in range(HALVES):
                with sp.Fori(0, BTILES) as btile:
                    for q in range(ROUNDS):
                        width = min(ROUND, VOCAB - q * ROUND)
                        sp.wait_ge(logits_free, PAIR_BUFFERS + half * SLOTS * PAIRS
                                   + btile * (ROUNDS * PAIRS) + (q + 1) * PAIRS)
                        sp.dma_start(y[half, btile, :, q * ROUND:q * ROUND + width],
                                     y_sb[:, btile * ROUNDS + q, 0:width]).then_inc(y_stored[q], 16)
            for q in range(ROUNDS):
                sp.wait_ge(y_stored[q], 16 * HALVES * BTILES)

        @block.gpsimd
        def _(pool):
            pool.memset(w_sb[:, FULL * D:TILES * D], 0.0).then_inc(w_tail_cleared, 1)
            pool.memset(ident[:, :], 0.0).then_inc(masks_cleared, 1)
            pool.memset(join[:, :], 0.0).then_inc(masks_cleared, 1)
            pool.wait_ge(masks_cleared, 2)
            pool.affine_select(out=ident[:, :], in_=ident[:, :], compare_op=ALU.not_equal, fill=1.0,
                               base=0, pattern=[[-1, P]], channel_multiplier=1).then_inc(masks_step, 1)
            join_v = join[:, :].rearrange("p (g d) -> p g d", g=PARTS)
            for g in range(GROUPS):
                pool.wait_ge(masks_step, g + 1)
                pool.affine_select(out=join_v, in_=join_v, compare_op=ALU.not_equal, fill=1.0,
                                   base=-g * D, pattern=[[0, PARTS], [-1, D]],
                                   channel_multiplier=1).then_inc(masks_step, 1)

        @block.tensor
        def _(pe):
            pe.sem_inc(w_parts_free, 1)
            turned = turned_ps[0:PARTS * D, :].bitcast(BF16)
            pe.wait_ge(masks_step, MASK_STEPS)
            with pe.Fori(0, ROUNDS) as n:
                pe.wait_ge(w_split, n * SPLIT_STEPS + SPLIT_STEPS)
                pe.wait_ge(turned_free, n + 1)
                for i in range(TURN):
                    last = nc.tensor.transpose(turned[:, i * P:(i + 1) * P], w_parts[:, i, :], ident[:, :])
                last.then_inc(w_parts_free, 1)

            with pe.Fori(0, HALVES) as half:
                for c in range(CHUNKS):
                    pe.wait_ge(x_loaded[c], (half + 1) * (16 * X_DMAS[c]))
                    for i in range(CHUNK):
                        t = c * CHUNK + i
                        g, rows = t % GROUPS, P if t < FULL else TAIL
                        last = nc.tensor.matmul(partial_ps[g * D:(g + 1) * D, 0:HB],
                                                w_sb[0:rows, t * D:(t + 1) * D],
                                                x_sb[0:rows, c, i * HB:(i + 1) * HB],
                                                start=t < GROUPS, stop=t >= TILES - GROUPS)
                    last.then_inc(x_free, 1)
                pe.wait_ge(partial_copied, half + 1)
                nc.tensor.matmul(total_ps[0:PARTS * D, 0:HB], join[:, :], partial_sb[:, :],
                                 start=True, stop=True).then_inc(total_ready, 1)
                pe.wait_ge(turned_free, ROUNDS + 1)
                with pe.Fori(0, BTILES) as btile:
                    pe.wait_ge(h_split, half * SPLIT_STEPS + SPLIT_STEPS)
                    for q in range(ROUNDS):
                        for pair in range(PAIRS):
                            pe.wait_ge(logits_free, half * (SLOTS * PAIRS) + btile * (ROUNDS * PAIRS)
                                       + (q * PAIRS + pair + 1))
                            for i in range(PAIR):
                                v = q * ROUND + (pair * PAIR + i) * BANK
                                for part in range(PARTS):
                                    last = nc.tensor.matmul(
                                        logits_ps[:, pair % PAIR_BUFFERS, i, :],
                                        h_parts[:, part, bass.ts(btile, P)], wT_parts[:, v:v + BANK],
                                        start=part == 0, stop=part == PARTS - 1)
                            last.then_inc(logits_ready, 1)

        @block.vector
        def _(dve):
            def split(whole, rest, parts, done, before):
                nc.vector.tensor_copy(parts[0], whole).then_inc(done, 1)
                dve.wait_ge(done, before + 1)
                nc.vector.tensor_tensor(rest, whole, parts[0], ALU.subtract).then_inc(done, 1)
                dve.wait_ge(done, before + 2)
                nc.vector.tensor_copy(parts[1], rest).then_inc(done, 1)
                dve.wait_ge(done, before + 3)
                nc.vector.tensor_tensor(parts[2], rest, parts[1], ALU.subtract).then_inc(done, 1)

            dve.wait_ge(w_loaded, 16)
            dve.wait_ge(w_tail_loaded, 16)
            with dve.Fori(0, ROUNDS) as n:
                dve.wait_ge(w_parts_free, n + 1)
                split(w_sb[:, bass.ts(n, TURN * D)].rearrange("p (t d) -> p t d", d=D), w_rest[:, :, :],
                      [w_parts[:, :, s * D:(s + 1) * D] for s in range(PARTS)],
                      w_split, n * SPLIT_STEPS)

            with dve.Fori(0, HALVES) as half:
                dve.wait_ge(x_free, half * CHUNKS + 2 * CHUNKS)
                nc.vector.tensor_copy(partial_sb[:, :], partial_ps[:, 0:HB]).then_inc(partial_copied, 1)
                dve.wait_ge(h_ready, half + 1)
                split(h_sb[:, :], h_rest[:, :], [h_parts[:, s, :] for s in range(PARTS)],
                      h_split, half * SPLIT_STEPS)

        @block.scalar
        def _(act):
            act.wait_ge(w_tail_cleared, 1)
            act.dma_start(w_sb[0:TAIL, FULL * D:TILES * D], w_tail[:, :]).then_inc(w_tail_loaded, 16)
            for g in range(PARTS):
                act.dma_start(bias_sb[g * D:(g + 1) * D, :], bias[:, :]).then_inc(bias_loaded, 16)
            act.sem_inc(turned_free, 1)
            act.sem_inc(logits_free, PAIR_BUFFERS)

            turned = turned_ps[0:PARTS * D, :].bitcast(BF16)
            with act.Fori(0, ROUNDS) as n:
                act.wait_ge(w_parts_free, n + 2)
                nc.scalar.activation(wT_parts[:, bass.ts(n, ROUND)], turned,
                                     ACT.Copy).then_inc(turned_free, 1)

            act.wait_ge(bias_loaded, 16 * PARTS)
            for half in range(HALVES):
                act.wait_ge(total_ready, half + 1)
                nc.scalar.activation(h_sb[:, :], total_ps[0:PARTS * D, 0:HB], ACT.Sigmoid,
                                     bias=bias_sb[:, 0:1]).then_inc(h_ready, 1)
                with act.Fori(0, BTILES) as btile:
                    for q in range(ROUNDS):
                        if half > 0:
                            act.wait_ge(y_stored[q], 16 * half * BTILES)
                        for pair in range(PAIRS):
                            act.wait_ge(logits_ready, half * SLOTS * PAIRS + btile * (ROUNDS * PAIRS)
                                        + (q * PAIRS + pair + 1))
                            nc.scalar.activation(
                                y_sb[:, btile * ROUNDS + q, pair * PAIR * BANK:(pair + 1) * PAIR * BANK],
                                logits_ps[:, pair % PAIR_BUFFERS, :, :],
                                ACT.Sigmoid).then_inc(logits_free, 1)


def kernel(r_x, L0_rec_w, L0_rec_b):
    import numpy as np
    import concourse.bacc as bacc
    from concourse.bass_utils import run_bass_kernel_spmd

    x, w, b = (np.asarray(a) for a in (r_x, L0_rec_w, L0_rec_b))
    x_main = x[:, :FULL * P].reshape(HALVES, HB, FULL, P).transpose(0, 3, 2, 1)
    x_tail = x[:, FULL * P:].reshape(HALVES, HB, TAIL).transpose(0, 2, 1)
    w_main = w[:FULL * P].reshape(FULL, P, D).transpose(1, 0, 2)
    arrays = {
        "x_main": np.ascontiguousarray(x_main).reshape(HALVES, P, FULL * HB),
        "x_tail": np.ascontiguousarray(x_tail),
        "w_main": np.ascontiguousarray(w_main).reshape(P, FULL * D),
        "w_tail": np.ascontiguousarray(w[FULL * P:]),
        "bias": b.reshape(D, 1),
    }
    nc = bacc.Bacc("TRN2", target_bir_lowering=False, num_devices=1)
    ins = [nc.dram_tensor(name, a.shape, F32, kind="ExternalInput").ap() for name, a in arrays.items()]
    y = nc.dram_tensor("y", (HALVES, BTILES, P, VOCAB), F32, kind="ExternalOutput").ap()
    autoencoder(nc, *ins, y)
    r = run_bass_kernel_spmd(nc, [arrays], core_ids=[0])
    return r.results[0]["y"].reshape(BATCH, VOCAB)
```

```python
from contextlib import ExitStack

import concourse.bass as bass
from concourse import mybir

P = 128
GROUPS = 4
D = 32
PARTS = 3
BATCH, VOCAB = 512, 10202
HALVES = 2
HB = BATCH // HALVES
TILES = -(-VOCAB // P)
FULL = TILES - 1
TAIL = VOCAB - FULL * P
CHUNK = 8
CHUNKS = TILES // CHUNK
BANK = 512
PAIR = 2
PAIR_BUFFERS = 2
ROUND = 2 * PAIR * BANK
ROUNDS = -(-VOCAB // ROUND)
PAIRS = ROUND // (PAIR * BANK)
TURN = 8
TURN_BUFFERS = 2
TURNS = TILES // TURN
BTILES = HB // P
SLOTS = BTILES * ROUNDS
SPLIT_STEPS = 4
assert CHUNKS * CHUNK == TILES == TURNS * TURN and TURNS % TURN_BUFFERS == 0

F32 = mybir.dt.float32
BF16 = mybir.dt.bfloat16
ALU = mybir.AluOpType
ACT = mybir.ActivationFunctionType


def autoencoder(nc, x_main, x_tail, w_main, w_tail, bias, y):
    with ExitStack() as ctx:
        def sb(name, shape, dt=F32):
            return ctx.enter_context(nc.sbuf_tensor(name, shape, dt))

        def psum(name, shape):
            return ctx.enter_context(nc.psum_tensor(name, shape, F32))

        def sem(name):
            return ctx.enter_context(nc.semaphore(name))

        x_sb = sb("x_sb", [P, CHUNKS, CHUNK * HB])
        y_sb = sb("y_sb", [P, SLOTS, ROUND])
        w_sb = sb("w_sb", [P, TILES * D])
        w_rest = sb("w_rest", [P, TURN_BUFFERS, TURN, D])
        w_parts = sb("w_parts", [P, TURN_BUFFERS, TURN, PARTS * D], BF16)
        wT_parts = sb("wT_parts", [PARTS * D, TILES * P], BF16)
        partial_sb = sb("partial_sb", [P, HB])
        h_sb = sb("h_sb", [PARTS * D, HB])
        h_rest = sb("h_rest", [PARTS * D, HB])
        h_parts = sb("h_parts", [PARTS * D, PARTS, HB], BF16)
        bias_sb = sb("bias_sb", [PARTS * D, 1])
        ident = sb("ident", [P, P], BF16)
        warm = sb("warm", [P, 1])
        join = sb("join", [P, PARTS * D])

        logits_ps = psum("logits_ps", [P, PAIR_BUFFERS, PAIR, BANK])
        turned_ps = psum("turned_ps", [P, TURN_BUFFERS, BANK])
        partial_ps = psum("partial_ps", [P, BANK])
        total_ps = psum("total_ps", [P, BANK])

        w_loaded = sem("w_loaded")
        w_tail_loaded = sem("w_tail_loaded")
        w_tail_cleared = sem("w_tail_cleared")
        bias_loaded = sem("bias_loaded")
        x_loaded = [sem(f"x_loaded{c}") for c in range(CHUNKS)]
        masks_cleared = sem("masks_cleared")
        masks_step = sem("masks_step")
        w_split = sem("w_split")
        w_parts_free = sem("w_parts_free")
        turned_free = sem("turned_free")
        x_free = sem("x_free")
        partial_copied = sem("partial_copied")
        total_ready = sem("total_ready")
        h_ready = sem("h_ready")
        h_split = sem("h_split")
        logits_ready = sem("logits_ready")
        logits_free = sem("logits_free")
        y_stored = [sem(f"y_stored{q}") for q in range(ROUNDS)]

        MASK_STEPS = 1 + GROUPS
        X_DMAS = [1] * (CHUNKS - 1) + [2]

        def turned(buf):
            return turned_ps[0:PARTS * D, buf, :].bitcast(BF16)

        block = ctx.enter_context(nc.Block())

        @block.sync
        def _(sp):
            sp.dma_start(w_sb[:, 0:FULL * D], w_main[:, :]).then_inc(w_loaded, 16)
            sp.sem_inc(x_free, CHUNKS)
            with sp.Fori(0, HALVES) as half:
                for c in range(CHUNKS):
                    sp.wait_ge(x_free, half * CHUNKS + (c + 1))
                    first, last = c * CHUNK, min((c + 1) * CHUNK, FULL)
                    sp.dma_start(x_sb[:, c, 0:(last - first) * HB],
                                 x_main[half, :, first * HB:last * HB]).then_inc(x_loaded[c], 16)
                sp.dma_start(x_sb[0:TAIL, CHUNKS - 1, (CHUNK - 1) * HB:CHUNK * HB],
                             x_tail[half, :, :]).then_inc(x_loaded[CHUNKS - 1], 16)
            with sp.Fori(0, HALVES) as half:
                with sp.Fori(0, BTILES) as btile:
                    for q in range(ROUNDS):
                        width = min(ROUND, VOCAB - q * ROUND)
                        sp.wait_ge(logits_free, half * (SLOTS * PAIRS) + btile * (ROUNDS * PAIRS)
                                   + (PAIR_BUFFERS + (q + 1) * PAIRS))
                        sp.dma_start(y[half, btile, :, q * ROUND:q * ROUND + width],
                                     y_sb[:, btile * ROUNDS + q, 0:width]).then_inc(y_stored[q], 16)
            for q in range(ROUNDS):
                sp.wait_ge(y_stored[q], 16 * HALVES * BTILES)

        @block.gpsimd
        def _(pool):
            pool.memset(w_sb[:, FULL * D:TILES * D], 0.0).then_inc(w_tail_cleared, 1)
            pool.memset(ident[:, :], 0.0).then_inc(masks_cleared, 1)
            pool.memset(join[:, :], 0.0).then_inc(masks_cleared, 1)
            pool.wait_ge(masks_cleared, 2)
            pool.affine_select(out=ident[:, :], in_=ident[:, :], compare_op=ALU.not_equal, fill=1.0,
                               base=0, pattern=[[-1, P]], channel_multiplier=1).then_inc(masks_step, 1)
            join_v = join[:, :].rearrange("p (g d) -> p g d", g=PARTS)
            for g in range(GROUPS):
                pool.wait_ge(masks_step, g + 1)
                pool.affine_select(out=join_v, in_=join_v, compare_op=ALU.not_equal, fill=1.0,
                                   base=-g * D, pattern=[[0, PARTS], [-1, D]],
                                   channel_multiplier=1).then_inc(masks_step, 1)

        @block.tensor
        def _(pe):
            pe.sem_inc(w_parts_free, TURN_BUFFERS)
            pe.wait_ge(masks_step, MASK_STEPS)
            with pe.Fori(0, TURNS // TURN_BUFFERS) as n:
                for buf in range(TURN_BUFFERS):
                    pe.wait_ge(w_split, n * (TURN_BUFFERS * SPLIT_STEPS) + (buf + 1) * SPLIT_STEPS)
                    pe.wait_ge(turned_free, n * TURN_BUFFERS + (buf + 1))
                    for i in range(TURN):
                        last = nc.tensor.transpose(turned(buf)[:, i * P:(i + 1) * P],
                                                   w_parts[:, buf, i, :], ident[:, :])
                    last.then_inc(w_parts_free, 1)

            with pe.Fori(0, HALVES) as half:
                for c in range(CHUNKS):
                    pe.wait_ge(x_loaded[c], (half + 1) * (16 * X_DMAS[c]))
                    for i in range(CHUNK):
                        t = c * CHUNK + i
                        g, rows = t % GROUPS, P if t < FULL else TAIL
                        last = nc.tensor.matmul(partial_ps[g * D:(g + 1) * D, 0:HB],
                                                w_sb[0:rows, t * D:(t + 1) * D],
                                                x_sb[0:rows, c, i * HB:(i + 1) * HB],
                                                start=t < GROUPS, stop=t >= TILES - GROUPS)
                    last.then_inc(x_free, 1)
                pe.wait_ge(partial_copied, half + 1)
                nc.tensor.matmul(total_ps[0:PARTS * D, 0:HB], join[:, :], partial_sb[:, :],
                                 start=True, stop=True).then_inc(total_ready, 1)
                pe.wait_ge(turned_free, TURN_BUFFERS + TURNS)
                with pe.Fori(0, BTILES) as btile:
                    pe.wait_ge(h_split, half * SPLIT_STEPS + SPLIT_STEPS)
                    for q in range(ROUNDS):
                        for pair in range(PAIRS):
                            pe.wait_ge(logits_free, half * (SLOTS * PAIRS) + btile * (ROUNDS * PAIRS)
                                       + (q * PAIRS + pair + 1))
                            for i in range(PAIR):
                                v = q * ROUND + (pair * PAIR + i) * BANK
                                for part in range(PARTS):
                                    last = nc.tensor.matmul(
                                        logits_ps[:, pair % PAIR_BUFFERS, i, :],
                                        h_parts[:, part, bass.ts(btile, P)], wT_parts[:, v:v + BANK],
                                        start=part == 0, stop=part == PARTS - 1)
                            last.then_inc(logits_ready, 1)

        @block.vector
        def _(dve):
            def split(whole, rest, parts, done, before):
                nc.vector.tensor_copy(parts[0], whole).then_inc(done, 1)
                dve.wait_ge(done, before + 1)
                nc.vector.tensor_tensor(rest, whole, parts[0], ALU.subtract).then_inc(done, 1)
                dve.wait_ge(done, before + 2)
                nc.vector.tensor_copy(parts[1], rest).then_inc(done, 1)
                dve.wait_ge(done, before + 3)
                nc.vector.tensor_tensor(parts[2], rest, parts[1], ALU.subtract).then_inc(done, 1)

            dve.wait_ge(w_loaded, 16)
            dve.wait_ge(w_tail_loaded, 16)
            with dve.Fori(0, TURNS // TURN_BUFFERS) as n:
                for buf in range(TURN_BUFFERS):
                    dve.wait_ge(w_parts_free, n * TURN_BUFFERS + (buf + 1))
                    split(w_sb[:, bass.ds(n * (TURN_BUFFERS * TURN * D) + buf * TURN * D, TURN * D)]
                          .rearrange("p (t d) -> p t d", d=D), w_rest[:, buf, :, :],
                          [w_parts[:, buf, :, s * D:(s + 1) * D] for s in range(PARTS)],
                          w_split, n * (TURN_BUFFERS * SPLIT_STEPS) + buf * SPLIT_STEPS)

            with dve.Fori(0, HALVES) as half:
                dve.wait_ge(x_free, half * CHUNKS + 2 * CHUNKS)
                nc.vector.tensor_copy(partial_sb[:, :], partial_ps[:, 0:HB]).then_inc(partial_copied, 1)
                dve.wait_ge(h_ready, half + 1)
                split(h_sb[:, :], h_rest[:, :], [h_parts[:, s, :] for s in range(PARTS)],
                      h_split, half * SPLIT_STEPS)

        @block.scalar
        def _(act):
            act.wait_ge(w_tail_cleared, 1)
            act.dma_start(w_sb[0:TAIL, FULL * D:TILES * D], w_tail[:, :]).then_inc(w_tail_loaded, 16)
            for g in range(PARTS):
                act.dma_start(bias_sb[g * D:(g + 1) * D, :], bias[:, :]).then_inc(bias_loaded, 16)
            act.sem_inc(turned_free, TURN_BUFFERS)
            act.sem_inc(logits_free, PAIR_BUFFERS)
            act.wait_ge(masks_step, MASK_STEPS)
            nc.scalar.activation(warm[:, :], join[:, 0:1], ACT.Sigmoid)

            with act.Fori(0, TURNS // TURN_BUFFERS) as n:
                for buf in range(TURN_BUFFERS):
                    act.wait_ge(w_parts_free, n * TURN_BUFFERS + (TURN_BUFFERS + buf + 1))
                    nc.scalar.activation(
                        wT_parts[:, bass.ds(n * (TURN_BUFFERS * TURN * P) + buf * TURN * P, TURN * P)],
                        turned(buf), ACT.Copy).then_inc(turned_free, 1)

            act.wait_ge(bias_loaded, 16 * PARTS)
            for half in range(HALVES):
                act.wait_ge(total_ready, half + 1)
                nc.scalar.activation(h_sb[:, :], total_ps[0:PARTS * D, 0:HB], ACT.Sigmoid,
                                     bias=bias_sb[:, 0:1]).then_inc(h_ready, 1)
                with act.Fori(0, BTILES) as btile:
                    for q in range(ROUNDS):
                        if half > 0:
                            act.wait_ge(y_stored[q], 16 * half * BTILES)
                        for pair in range(PAIRS):
                            act.wait_ge(logits_ready, half * SLOTS * PAIRS + btile * (ROUNDS * PAIRS)
                                        + (q * PAIRS + pair + 1))
                            nc.scalar.activation(
                                y_sb[:, btile * ROUNDS + q, pair * PAIR * BANK:(pair + 1) * PAIR * BANK],
                                logits_ps[:, pair % PAIR_BUFFERS, :, :],
                                ACT.Sigmoid).then_inc(logits_free, 1)


def kernel(r_x, L0_rec_w, L0_rec_b):
    import numpy as np
    import concourse.bacc as bacc
    from concourse.bass_utils import run_bass_kernel_spmd

    x, w, b = (np.asarray(a) for a in (r_x, L0_rec_w, L0_rec_b))
    x_main = x[:, :FULL * P].reshape(HALVES, HB, FULL, P).transpose(0, 3, 2, 1)
    x_tail = x[:, FULL * P:].reshape(HALVES, HB, TAIL).transpose(0, 2, 1)
    w_main = w[:FULL * P].reshape(FULL, P, D).transpose(1, 0, 2)
    arrays = {
        "x_main": np.ascontiguousarray(x_main).reshape(HALVES, P, FULL * HB),
        "x_tail": np.ascontiguousarray(x_tail),
        "w_main": np.ascontiguousarray(w_main).reshape(P, FULL * D),
        "w_tail": np.ascontiguousarray(w[FULL * P:]),
        "bias": b.reshape(D, 1),
    }
    nc = bacc.Bacc("TRN2", target_bir_lowering=False, num_devices=1)
    ins = [nc.dram_tensor(name, a.shape, F32, kind="ExternalInput").ap() for name, a in arrays.items()]
    y = nc.dram_tensor("y", (HALVES, BTILES, P, VOCAB), F32, kind="ExternalOutput").ap()
    autoencoder(nc, *ins, y)
    r = run_bass_kernel_spmd(nc, [arrays], core_ids=[0])
    return r.results[0]["y"].reshape(BATCH, VOCAB)
```
